# Optimizing a Trainium2 kernel written in Bass

```python
import numpy as np
import jax
import jax.numpy as jnp

def _softmax(x, axis=-1):
    return jax.nn.softmax(x, axis=axis)
def _gelu(x):
    return jax.nn.gelu(x, approximate=True)
def _silu(x):
    return jax.nn.silu(x)
def _sigmoid(x):
    return jax.nn.sigmoid(x)
def _layernorm(x, axis=-1, eps=1e-5):
    m = jnp.mean(x, axis=axis, keepdims=True)
    v = jnp.var(x, axis=axis, keepdims=True)
    return (x - m) / jnp.sqrt(v + eps)
def _scatter_add(tgt, idx, src, axis=0):
    return tgt.at[idx].add(src)
def _segment_sum(src, seg, n):
    return jax.ops.segment_sum(src, seg, n)

kernel_name = 'mk_adj_preln_d1_adj_256_d006ec'

def setup_inputs(seed: int = 0):
    np.random.seed(seed)
    _w = jnp.asarray
    def _rec_inputs():
        import jax
        import jax.numpy as jnp
        _gk = jax.random.key(seed)
        x = -0.000929 + 1 * jax.random.normal(jax.random.fold_in(_gk, 1), (8192, 256), jnp.float32)
        _a = jax.random.bernoulli(jax.random.fold_in(_gk, 2), 0.00390625, (8192, 8192))
        _a = jnp.logical_or(_a, jnp.swapaxes(_a, -1, -2))
        _a = jnp.logical_or(_a, jnp.eye(8192, dtype=bool))
        _af = _a.astype(jnp.float32)
        _af = _af * jax.random.uniform(jax.random.fold_in(_gk, 3), (8192, 8192), jnp.float32, 0.05, 1)
        adj = _af
        return x, adj
    x, adj = _rec_inputs()
    def _L0_gnn_setup():
        import jax, jax.numpy as jnp
        import numpy as np
        N = 4096
        IN = 256
        H = 8
        D = 32
        ALPHA = 0.2
        key = jax.random.key(seed)
        ks = jax.random.split(key, 9)
        xav = lambda k, sh: jax.random.normal(k, sh, jnp.float32) * np.float32(np.sqrt(2.0 / (sh[0] + sh[-1])))
        return {'x': jax.random.normal(ks[0], (N, IN), jnp.float32), 'adj_matrix': jax.random.uniform(ks[1], (N, N), jnp.float32), 'W': xav(ks[2], (H * D, IN)), 'We': xav(ks[3], (H, 1)), 'be': jnp.zeros((H,), jnp.float32), 'a_src': xav(ks[4], (H, D)), 'a_dst': xav(ks[5], (H, D)), 'Wr': xav(ks[6], (H * D, IN)), 'br': jnp.zeros((H * D,), jnp.float32)}
    _L0_gnn_all = _L0_gnn_setup()
    _L0_gnn_in = {k: v for k, v in _L0_gnn_all.items() if k in ('W', 'We', 'be', 'a_src', 'a_dst', 'Wr', 'br', )}
    del _L0_gnn_all

    return {
        "x": x,
        "adj": adj,
        "L0_gnn_W": _L0_gnn_in["W"],
        "L0_gnn_We": _L0_gnn_in["We"],
        "L0_gnn_be": _L0_gnn_in["be"],
        "L0_gnn_a_src": _L0_gnn_in["a_src"],
        "L0_gnn_a_dst": _L0_gnn_in["a_dst"],
        "L0_gnn_Wr": _L0_gnn_in["Wr"],
        "L0_gnn_br": _L0_gnn_in["br"],
    }

def reference(x, adj, L0_gnn_W, L0_gnn_We, L0_gnn_be, L0_gnn_a_src, L0_gnn_a_dst, L0_gnn_Wr, L0_gnn_br):
    import jax
    import jax.numpy as jnp
    def _L0_gnn_ref(x, adj_matrix, W, We, be, a_src, a_dst, Wr, br):
        import jax, jax.numpy as jnp
        import numpy as np
        N = 4096
        IN = 256
        H = 8
        D = 32
        ALPHA = 0.2
        n = x.shape[0]
        h = (x @ W.T).reshape(n, H, D)
        s_src = jnp.einsum('nhd,hd->nh', h, a_src)
        s_dst = jnp.einsum('nhd,hd->nh', h, a_dst)
        attn = s_src[:, None, :] + s_dst[None, :, :]
        attn = attn + adj_matrix[:, :, None] * We[:, 0] + be
        mask = (adj_matrix > 0)[:, :, None]
        attn = jnp.where(mask, attn, -jnp.inf)
        attn = jax.nn.leaky_relu(attn, ALPHA)
        attn = jax.nn.softmax(attn, axis=1)
        h_out = jnp.einsum('ijh,jhd->ihd', attn, h).reshape(n, H * D)
        return h_out + x @ Wr.T + br

    h = jnp.maximum(_layernorm(x, axis=-1), 0.0)
    x = x + _L0_gnn_ref(h, adj, L0_gnn_W, L0_gnn_We, L0_gnn_be, L0_gnn_a_src, L0_gnn_a_dst, L0_gnn_Wr, L0_gnn_br)
    return x


_drawn_inputs = setup_inputs


def setup_inputs(seed=0):
    import zlib

    import numpy as np

    out = dict(_drawn_inputs(seed))
    spreads = {'L0_gnn_be': (0.0, 0.8), 'L0_gnn_br': (0.0, 0.1)}
    factors = {'L0_gnn_We': 4.996, 'L0_gnn_a_src': 3.188}
    for name, (base, spread) in spreads.items():
        noise = np.random.default_rng([zlib.crc32(name.encode()), seed]).standard_normal(out[name].shape)
        drawn = base * np.exp(spread * noise) if base else spread * noise
        out[name] = jnp.asarray(drawn.astype(out[name].dtype))
    for name, factor in factors.items():
        out[name] = (out[name] * factor).astype(out[name].dtype)
    return out
```

```python
import concourse.bass as bass
from concourse import mybir
from contextlib import ExitStack

F32 = mybir.dt.float32
BF16 = mybir.dt.bfloat16
I32 = mybir.dt.int32
ALU = mybir.AluOpType
ACT = mybir.ActivationFunctionType
AX = mybir.AxisListType
RMAX = bass.bass_isa.ReduceOp.max

P = 128
N, C = 8192, 256
H, D = 8, 32
CK = C // P
SLOPE = 0.2
EPS = 1e-5
T = N // P

IB = 1024
NIB = N // IB
NI = IB // P
JT = 2
JC = JT * P
NQ = N // JC
SLOTS = 4
RAW = 2
RING = 4
U = H
POOL_ADD = (1, 2, 4, 5, 7)
NPA = len(POOL_ADD)
NDA = H - NPA
LAG = 2
HW = D + 1
HX = H * HW + H
BIG = 2.0 ** 100
TINY = 2.0 ** -70
LO, HI = 1e-30, 1e25
PER_BANK = 512 // HW
BLOCKS = NI * H
OBANKS = -(-BLOCKS // PER_BANK)


def gat_layer(nc, x, adj, W, We, be, a_src, a_dst, Wr, br, out):
    ctx = ExitStack()
    with ctx:
        def sb(name, shape, dt=F32):
            return ctx.enter_context(nc.sbuf_tensor(name, shape, dt))

        def sem(name):
            return ctx.enter_context(nc.semaphore(name))

        table_dram = nc.dram_tensor("table_dram", [N, HX], F32).ap()
        resid_dram = nc.dram_tensor("resid_dram", [N, C], F32).ap()
        ssrc_dram = nc.dram_tensor("ssrc_dram", [H, N], F32).ap()

        raw = sb("raw", [P, RAW, NI, JC])
        pen = sb("pen", [P, NI, JC], BF16)
        adjT = sb("adjT", [P, 2, 2, JT, IB])
        zs = sb("zs", [P, RING, JT, IB])
        ps = sb("ps", [P, RING, JT, IB])
        srow = sb("srow", [P, 2, H, IB])
        table = sb("table", [P, SLOTS, JT, HX])
        resid = sb("resid", [P, NI, C])
        result = sb("result", [P, NI, C])
        rsum = sb("rsum", [P, BLOCKS])
        inlo = sb("inlo", [P, BLOCKS])
        inrange = sb("inrange", [P, BLOCKS])
        fine = sb("fine", [P, BLOCKS])
        eye = sb("eye", [P, P])
        zeros = sb("zeros", [P, 512], BF16)
        w_all = sb("w_all", [P, H])
        w_mag = sb("w_mag", [P, H])
        w_abs = sb("w_abs", [P, H])
        w_sgn = sb("w_sgn", [P, H])
        w_neg = sb("w_neg", [P, H], I32)
        be_all = sb("be_all", [P, H])
        smax = sb("smax", [P, 2 * H])
        smax_all = sb("smax_all", [P, 2 * H])
        most = sb("most", [P, H])
        most_be = sb("most_be", [P, H])
        most_relu = sb("most_relu", [P, H])
        shift = sb("shift", [P, H])

        xs = srow[:, :, :, :].rearrange("p a h i -> p (a h i)").rearrange("p (t c) -> p t c", c=C)
        pool = ps[:, :, :, :].rearrange("p s j i -> p (s j i)")
        used = [0]

        def part(n):
            used[0] += n
            assert used[0] <= RING * JT * IB
            return pool[:, used[0] - n:used[0]]

        wsb = part(2 * CK * C).rearrange("p (m o k) -> p m o k", m=2, o=CK)
        amat = part(CK * 2 * H).rearrange("p (o m) -> p o m", o=CK)
        acol = part(CK * 2).rearrange("p (o m) -> p o m", o=CK)
        wall = part(CK * (2 * C + 2 * H)).rearrange("p (k n) -> p k n", k=CK)
        br_all = part(C)
        stats = part(T * 6).rearrange("p (t s) -> p t s", s=6)
        mv = part(T * 2).rearrange("p (t s) -> p t s", s=2)
        rstd = part(T)
        nmr = part(T)
        xn = part(2 * C).rearrange("p (s c) -> p s c", s=2)
        xb = part(2 * C).rearrange("p (s c) -> p s c", s=2)
        hnT = part(2 * CK * P).rearrange("p (s k i) -> p s k i", s=2, k=CK)
        tt = part(2 * H).rearrange("p (s h) -> p s h", s=2)
        et = part(2 * H).rearrange("p (s h) -> p s h", s=2)
        tab = part(2 * HX).rearrange("p (s n) -> p s n", s=2)
        rs = part(2 * C).rearrange("p (s c) -> p s c", s=2)
        ssT = part(2 * P).rearrange("p (s c) -> p s c", s=2)

        banks = [ctx.enter_context(nc.psum_tensor(f"bank{i}", [P, 512], F32)) for i in range(8)]
        OB, TB = banks[:OBANKS], banks[OBANKS:OBANKS + 2]
        flip, projA, projB = banks[0:2], banks[2:4], banks[4:6]

        consts_ready = sem("consts_ready")
        eye_zero = sem("eye_zero")
        amat_zero = sem("amat_zero")
        w_here = sem("w_here")
        small_here = sem("small_here")
        x_here = sem("x_here")
        amat_ready = sem("amat_ready")
        wsgn_step = sem("wsgn_step")
        wT_done = sem("wT_done")
        wT_kept = sem("wT_kept")
        stat_done = sem("stat_done")
        aggr_done = sem("aggr_done")
        rstd_done = sem("rstd_done")
        norm_ready = sem("norm_ready")
        xn_ready = sem("xn_ready")
        xb_ready = sem("xb_ready")
        xn_free = sem("xn_free")
        flip_done = sem("flip_done")
        hnT_ready = sem("hnT_ready")
        proj_done = sem("proj_done")
        proj_read = sem("proj_read")
        t_ready = sem("t_ready")
        et_ready = sem("et_ready")
        tab_ready = sem("tab_ready")
        stored = sem("stored")
        smax_step = sem("smax_step")
        smax_ready = sem("smax_ready")
        smax_spread = sem("smax_spread")
        shift_step = sem("shift_step")
        shift_ready = sem("shift_ready")
        adj_here = [sem(f"adj_here{s}") for s in range(RAW)]
        table_here = [sem(f"table_here{s}") for s in range(SLOTS)]
        step_free = sem("step_free")
        pen_ready = sem("pen_ready")
        masked = sem("masked")
        tb_filled = sem("tb_filled")
        tb_free = sem("tb_free")
        folded = sem("folded")
        srow_here = [sem(f"srow_here{b}") for b in range(2)]
        resid_here = sem("resid_here")
        z_ready = sem("z_ready")
        relu_ready = sem("relu_ready")
        sum_dve = sem("sum_dve")
        sum_pool = sem("sum_pool")
        p_ready = sem("p_ready")
        p_free = sem("p_free")
        acc_free = sem("acc_free")
        rsum_ready = sem("rsum_ready")
        scaled = sem("scaled")
        result_ready = sem("result_ready")
        range_step = sem("range_step")
        out_done = sem("out_done")

        def block_ap(b):
            return OB[b // PER_BANK][:, (b % PER_BANK) * HW:(b % PER_BANK + 1) * HW]

        def bank_blocks(k):
            return PER_BANK * k, min(BLOCKS, PER_BANK * (k + 1))

        def blocks_of_rows():
            return

        block = ctx.enter_context(nc.Block())

        @block.sync
        def _(sp):
            sp.dma_start(wsb[:, 0], W.rearrange("(o p) k -> p o k", p=P)).then_inc(w_here, 16)
            sp.dma_start(wsb[:, 1], Wr.rearrange("(o p) k -> p o k", p=P)).then_inc(w_here, 16)
            sp.dma_start(acol[:, :, 0], a_dst.rearrange("(o g) d -> (g d) o", o=CK),
                         allow_slow_non_contiguous=True).then_inc(small_here, 16)
            sp.dma_start(acol[:, :, 1], a_src.rearrange("(o g) d -> (g d) o", o=CK),
                         allow_slow_non_contiguous=True).then_inc(small_here, 16)
            sp.dma_start(w_all[:, :], We.rearrange("h a -> a h").partition_broadcast(P)).then_inc(small_here, 16)
            sp.dma_start(be_all[:, :], be.partition_broadcast(P)).then_inc(small_here, 16)
            sp.dma_start(br_all[:, :], br.partition_broadcast(P)).then_inc(small_here, 16)
            for g in range(8):
                n = T // 8
                sp.dma_start(xs[:, g * n:(g + 1) * n, :],
                             x[g * n * P:(g + 1) * n * P, :].rearrange("(t p) c -> p t c", p=P)).then_inc(x_here, 16)
            with sp.Fori(0, T // 2) as it:
                for k in range(2):
                    t = it * 2 + k
                    sp.wait_ge(tab_ready, t + 1)
                    sp.dma_start(table_dram[bass.ds(t * P, P), :], tab[:, k, :]).then_inc(stored, 16)
                    sp.dma_start(resid_dram[bass.ds(t * P, P), :], rs[:, k, :]).then_inc(stored, 16)
                    sp.dma_start(ssrc_dram[:, bass.ds(t * P, P)], ssT[0:H, k, :]).then_inc(stored, 16)
            sp.wait_ge(stored, 16 * 3 * T + 16)

            def load_adj(ib, jq, q, s):
                sp.wait_ge(tb_filled, (q + 1) * (2 * JT))
                sp.dma_start(raw[:, s % RAW], adj[bass.ds(ib * IB, IB), bass.ds(jq * JC, JC)]
                             .rearrange("(n p) j -> p n j", p=P)).then_inc(adj_here[s % RAW], 16)

            def load_table(jq, q, s):
                sp.wait_ge(step_free, q + 1)
                sp.dma_start(table[:, s], table_dram[bass.ds(jq * JC, JC), :]
                             .rearrange("(n p) c -> p n c", p=P)).then_inc(table_here[s], 16)

            with sp.Fori(0, NIB) as ib:
                with sp.Fori(0, NQ // SLOTS) as it:
                    for s in range(SLOTS):
                        load_adj(ib, it * SLOTS + s, ib * NQ + it * SLOTS + s, s)
                        load_table(it * SLOTS + s, ib * NQ + it * SLOTS + s, s)
            load_adj(0, 0, NIB * NQ, 0)
            sp.wait_ge(adj_here[0], (NIB * NQ // RAW + 1) * 16)
            sp.wait_ge(srow_here[0], (NIB // 2 + 1) * 16)
            sp.wait_ge(out_done, 16 * NIB + 16)

        @block.gpsimd
        def _(gp):
            gp.memset(eye[:, :], 0.0).then_inc(eye_zero, 1)
            gp.memset(zeros[:, :], 0.0).then_inc(consts_ready, 1)
            gp.memset(amat[:, :, :], 0.0).then_inc(amat_zero, 1)
            gp.wait_ge(eye_zero, 1)
            gp.affine_select(out=eye[:, :], in_=eye[:, :], compare_op=ALU.not_equal, fill=1.0, base=0,
                             pattern=[[-1, P]], channel_multiplier=1).then_inc(consts_ready, 1)
            gp.wait_ge(x_here, 16 * 8)
            gp.wait_ge(small_here, 16 * 5)
            with gp.Fori(0, T // 2) as it:
                for k in range(2):
                    t = it * 2 + k
                    gp.wait_ge(proj_read, t + 1)
                    gp.tensor_tensor(xb[:, k, :], xs[:, bass.ds(t, 1), :].rearrange("p a c -> p (a c)"),
                                     br_all[:, :], ALU.add).then_inc(xb_ready, 1)
            gp.wait_ge(smax_ready, 1)
            gp.partition_all_reduce(smax_all[:, :], smax[:, :], P, RMAX).then_inc(smax_spread, 1)

            def mask(q, s):
                gp.wait_ge(pen_ready, q + 1)
                gp.tensor_tensor(raw[:, s % RAW], raw[:, s % RAW], pen[:, :, :], ALU.add).then_inc(masked, 1)

            gp.sem_inc(sum_pool, NPA)
            mask(0, 0)
            with gp.Fori(0, NIB * NQ // SLOTS) as g:
                for s in range(SLOTS):
                    for h in range(H):
                        if h == 0:
                            mask(g * SLOTS + s + 1, (s + 1) % SLOTS)
                        if h in POOL_ADD:
                            w = s * U + h
                            gp.wait_ge(relu_ready, g * (SLOTS * U) + w + 1)
                            gp.tensor_tensor(ps[:, w % RING], zs[:, w % RING], ps[:, w % RING], ALU.add)\
                              .then_inc(sum_pool, 1)

        @block.scalar
        def _(act):
            act.wait_ge(wT_done, 1)
            for k in range(CK):
                nc.scalar.activation(wall[:, k, 0:C], flip[0][:, k * C:(k + 1) * C], ACT.Copy)
                nc.scalar.activation(wall[:, k, C + 2 * H:], flip[1][:, k * C:(k + 1) * C], ACT.Copy)
                nc.scalar.activation(wall[:, k, C:C + 2 * H], projA[0][:, k * 2 * H:(k + 1) * 2 * H],
                                     ACT.Copy).then_inc(wT_kept, 1)
            act.wait_ge(rstd_done, 1)
            nc.scalar.activation(rstd[:, :], nmr[:, :], ACT.Sqrt).then_inc(rstd_done, 1)
            act.wait_ge(norm_ready, 1)
            with act.Fori(0, T // 2) as it:
                for k in range(2):
                    t = it * 2 + k
                    act.wait_ge(xn_free, t + 1)
                    act.wait_ge(norm_ready, 1)
                    nc.scalar.activation(xn[:, k, :], xs[:, bass.ds(t, 1), :].rearrange("p a c -> p (a c)"),
                                         ACT.Relu, bias=nmr[:, bass.ds(t, 1)],
                                         scale=rstd[:, bass.ds(t, 1)]).then_inc(xn_ready, 1)
                    act.wait_ge(proj_read, t + 1)
                    act.wait_ge(flip_done, t + 1)
                    nc.scalar.activation(hnT[:, k], flip[k][:, 0:C].rearrange("p (k i) -> p k i", k=CK),
                                         ACT.Copy).then_inc(hnT_ready, 1)
                    act.wait_ge(t_ready, t + 1)
                    nc.scalar.activation(et[:, k, :], tt[:, k, :], ACT.Exp, scale=SLOPE).then_inc(et_ready, 1)
            act.wait_ge(stored, 16 * 3 * T + 16)
            act.wait_ge(xn_ready, T)
            act.wait_ge(xb_ready, T)

            def load_srow(ib, b):
                act.dma_start(srow[:, b], ssrc_dram[:, bass.ds(ib * IB, IB)].partition_broadcast(P))\
                   .then_inc(srow_here[b], 16)

            load_srow(0, 0)
            act.wait_ge(shift_ready, 1)

            def relu(g, u, w):
                s, h = w // U, w % U
                act.wait_ge(p_free, u + 1)
                if h == 0:
                    act.wait_ge(table_here[s], g * 16 + 16)
                act.wait_ge(z_ready, u + 1)
                for j in range(JT):
                    ins = nc.scalar.activation(ps[:, w % RING, j], zs[:, w % RING, j], ACT.Relu, scale=(1.0 - SLOPE) / SLOPE,
                                               bias=table[:, s, j, H * HW + h:H * HW + h + 1])
                ins.then_inc(relu_ready, 1)

            def exp(g, w):
                s, h = w // U, w % U
                q = g * SLOTS + s
                if h in POOL_ADD:
                    act.wait_ge(sum_pool, q * NPA + sum(m <= h for m in POOL_ADD) + NPA)
                else:
                    act.wait_ge(sum_dve, q * NDA + h + 1 - sum(m <= h for m in POOL_ADD) + NDA)
                nc.scalar.activation(ps[:, w % RING], ps[:, w % RING], ACT.Exp, bias=shift[:, h:h + 1])\
                  .then_inc(p_ready, 1)

            with act.Fori(0, NIB // 2) as io:
                for b in range(2):
                    ib = io * 2 + b
                    load_srow((ib + 1) % NIB if b else ib + 1, 1 - b)
                    act.dma_start(resid[:, :, :], resid_dram[bass.ds(ib * IB, IB), :]
                                  .rearrange("(n p) c -> p n c", p=P)).then_inc(resid_here, 16)
                    with act.Fori(0, NQ // SLOTS) as it:
                        g = ib * (NQ // SLOTS) + it
                        for w in range(SLOTS * U):
                            relu(g, g * (SLOTS * U) + w, w)
                            if w >= LAG:
                                exp(g, w - LAG)
                        for w in range(SLOTS * U - LAG, SLOTS * U):
                            exp(g, w)
                    act.wait_ge(result_ready, ib + 1)
                    act.dma_start(out[bass.ds(ib * IB, IB), :].rearrange("(n p) c -> p n c", p=P),
                                  result[:, :, :]).then_inc(out_done, 16)

        @block.vector
        def _(dve):
            v = nc.vector
            dve.sem_inc(proj_read, 2)
            dve.sem_inc(tb_free, 2)
            dve.sem_inc(acc_free, 1)
            dve.sem_inc(sum_dve, NDA)
            dve.sem_inc(stored, 16)
            dve.sem_inc(out_done, 16)
            dve.sem_inc(range_step, 3)
            v.memset(fine[:, :], 1.0)
            v.memset(smax[:, :], -3.0e38).then_inc(smax_step, 1)
            dve.wait_ge(small_here, 16 * 5)
            dve.wait_ge(amat_zero, 1)
            for o in range(CK):
                for g in range(P // D):
                    for m in range(2):
                        h = o * (P // D) + g
                        ins = v.tensor_copy(amat[g * D:(g + 1) * D, o, m * H + h:m * H + h + 1],
                                            acol[g * D:(g + 1) * D, o, m:m + 1])
            ins.then_inc(amat_ready, 1)
            v.tensor_scalar(w_neg[:, :], w_all[:, :], 0.0, None, ALU.is_lt)
            v.tensor_scalar(w_sgn[:, :], w_all[:, :], 0.0, 2.0 * SLOPE, ALU.is_ge, ALU.mult)
            v.scalar_tensor_tensor(w_abs[:, :], w_all[:, :], -1.0, w_all[:, :], ALU.mult, ALU.max)\
             .then_inc(wsgn_step, 1)
            dve.wait_ge(wsgn_step, 1)
            v.tensor_scalar(w_mag[:, :], w_abs[:, :], TINY, None, ALU.max).then_inc(wsgn_step, 1)
            dve.wait_ge(wsgn_step, 2)
            v.scalar_tensor_tensor(w_all[:, :], w_sgn[:, :], -SLOPE, w_mag[:, :], ALU.add, ALU.mult)\
             .then_inc(wsgn_step, 1)
            dve.wait_ge(x_here, 16 * 8)
            for t in range(T):
                v.bn_stats(stats[:, t, :], xs[:, t, :]).then_inc(stat_done, 1)
            for t in range(T):
                dve.wait_ge(stat_done, t + 1)
                v.bn_aggr(mv[:, t, :], stats[:, t, :]).then_inc(aggr_done, 1)
            dve.wait_ge(aggr_done, T)
            v.tensor_scalar(nmr[:, :], mv[:, :, 1], EPS, None, ALU.add).then_inc(rstd_done, 1)
            dve.wait_ge(rstd_done, 2)
            v.reciprocal(rstd[:, :], rstd[:, :]).then_inc(rstd_done, 1)
            dve.wait_ge(rstd_done, 3)
            v.scalar_tensor_tensor(nmr[:, :], mv[:, :, 0], -1.0, rstd[:, :], ALU.mult, ALU.mult)\
             .then_inc(norm_ready, 1)
            with dve.Fori(0, T // 2) as it:
                for k in range(2):
                    t = it * 2 + k
                    dve.wait_ge(proj_done, t + 1)
                    dve.wait_ge(stored, 16 * 3 * t + 16)
                    dve.wait_ge(xb_ready, t + 1)
                    dve.wait_ge(smax_step, t + 1)
                    v.tensor_tensor(tt[:, k, :], projA[k][:, C:C + H], be_all[:, :], ALU.add).then_inc(t_ready, 1)
                    v.tensor_tensor(smax[:, :], projA[k][:, C:C + 2 * H], smax[:, :], ALU.max).then_inc(smax_step, 1)
                    v.tensor_scalar(ssT[0:H, k, :], projB[k][0:H, C:C + P], SLOPE, None, ALU.mult)
                    dve.wait_ge(t_ready, t + 1)
                    v.tensor_scalar(tab[:, k, H * HW:], tt[:, k, :], 1.0 - SLOPE, None, ALU.mult)
                    dve.wait_ge(et_ready, t + 1)
                    heads = tab[:, k, 0:H * HW].rearrange("p (h d) -> p h d", h=H)
                    v.tensor_tensor(heads[:, :, 0:D], projA[k][:, 0:C].rearrange("p (h d) -> p h d", h=H),
                                    et[:, k, :].unsqueeze(2).to_broadcast([P, H, D]), ALU.mult)
                    v.tensor_copy(heads[:, :, D], et[:, k, :])
                    v.tensor_tensor(rs[:, k, :], projB[k][:, 0:C], xb[:, k, :], ALU.add).then_inc(tab_ready, 1)
                    dve.wait_ge(tab_ready, t + 1)
                    dve.sem_inc(proj_read, 1)
            dve.wait_ge(smax_step, T + 1)
            dve.sem_inc(smax_ready, 1)
            dve.wait_ge(smax_spread, 1)
            v.tensor_tensor(most[:, :], smax_all[:, 0:H], smax_all[:, H:], ALU.add).then_inc(shift_step, 1)
            dve.wait_ge(shift_step, 1)
            v.tensor_tensor(most_be[:, :], most[:, :], be_all[:, :], ALU.add).then_inc(shift_step, 1)
            dve.wait_ge(shift_step, 2)
            v.tensor_scalar(most_relu[:, :], most_be[:, :], 0.0, SLOPE - 1.0, ALU.max, ALU.mult).then_inc(shift_step, 1)
            dve.wait_ge(shift_step, 3)
            v.scalar_tensor_tensor(shift[:, :], smax_all[:, H:], -SLOPE, most_relu[:, :], ALU.mult, ALU.add)\
             .then_inc(shift_ready, 1)

            dve.wait_ge(wsgn_step, 3)
            which = [v.value_load(w_neg[0:1, h:h + 1], min_val=0, max_val=1) for h in range(H)]

            def penalise(q, s, n, first=False):
                dve.wait_ge(adj_here[s % RAW], n)
                if not first:
                    dve.wait_ge(masked, q)
                v.tensor_scalar(pen[:, :, :], raw[:, s % RAW], 0.0, -BIG, ALU.is_le, ALU.mult).then_inc(pen_ready, 1)

            def take_sum(g, w):
                dve.wait_ge(relu_ready, g * (SLOTS * U) + w + 1)
                v.tensor_tensor(ps[:, w % RING], zs[:, w % RING], ps[:, w % RING], ALU.add).then_inc(sum_dve, 1)

            def keep(f, a, n):
                dve.wait_ge(tb_filled, f + 1 + RAW * 2 * JT)
                j, half = n // 2, n % 2
                at = slice(half * 512, half * 512 + 512)
                v.tensor_copy(adjT[:, a, 0, j, at], TB[n % 2][:, :]).then_inc(tb_free, 1)

            def fold(q, a):
                dve.wait_ge(tb_free, (q + 1) * (2 * JT) + 2)
                v.scalar_tensor_tensor(adjT[:, a, 1], adjT[:, a, 0], -1.0, adjT[:, a, 0], ALU.mult, ALU.max)\
                 .then_inc(folded, 1)

            penalise(0, 0, 16, first=True)
            for n in range(2 * JT):
                keep(n, 0, n)
            fold(0, 0)
            with dve.Fori(0, NIB // 2) as io:
                for b in range(2):
                    ib = io * 2 + b
                    with dve.Fori(0, NQ // SLOTS) as it:
                        g = ib * (NQ // SLOTS) + it
                        for s in range(SLOTS):
                            dve.wait_ge(srow_here[b], io * 16 + 16)
                            penalise(g * SLOTS + s + 1, (s + 1) % SLOTS,
                                     (g * SLOTS + s + 1 - (s + 1) % RAW) * (16 // RAW) + 16)
                            dve.wait_ge(folded, g * SLOTS + s + 1)
                            for h in range(H):
                                w = s * U + h
                                q = g * SLOTS + s
                                last = (h - RING) % U
                                n = sum(m <= last for m in POOL_ADD)
                                if last in POOL_ADD:
                                    dve.wait_ge(sum_pool, q * NPA + n + (NPA if h >= RING else 0))
                                else:
                                    dve.wait_ge(sum_dve, q * NDA + last + 1 - n + (NDA if h >= RING else 0))
                                v.scalar_tensor_tensor(
                                    zs[:, w % RING],
                                    adjT[:, s % 2, bass.ds(which[h], 1)].rearrange("p a j i -> p (a j) i"),
                                    w_all[:, h:h + 1],
                                    srow[:, b, h, :].unsqueeze(1).to_broadcast([P, JT, IB]),
                                    ALU.mult, ALU.add).then_inc(z_ready, 1)
                                if h >= RING:
                                    n = h - RING
                                    dve.wait_ge(z_ready, q * U + 1)
                                    keep((q + 1) * (2 * JT) + n, (s + 1) % 2, n)
                                if h and h - 1 not in POOL_ADD:
                                    take_sum(g, w - 1)
                                if h == U - 1 and h not in POOL_ADD:
                                    take_sum(g, w)
                            fold(g * SLOTS + s + 1, (s + 1) % 2)
                    dve.wait_ge(p_free, (ib + 1) * (NQ * U) + RING)
                    dve.wait_ge(range_step, ib * 3 + 3)
                    for k in range(OBANKS):
                        lo, hi = bank_blocks(k)
                        acc = OB[k][:, 0:(hi - lo) * HW].rearrange("p (b w) -> p b w", w=HW)
                        v.reciprocal(rsum[:, lo:hi], acc[:, :, D]).then_inc(rsum_ready, 1)
                    dve.wait_ge(out_done, ib * 16 + 16)
                    for k in range(OBANKS):
                        lo, hi = bank_blocks(k)
                        acc = OB[k][:, 0:(hi - lo) * HW].rearrange("p (b w) -> p b w", w=HW)
                        dve.wait_ge(rsum_ready, ib * OBANKS + k + 1)
                        ins = v.tensor_tensor(
                            result[:, :, :].rearrange("p n (h d) -> p (n h) d", h=H)[:, lo:hi, :],
                            acc[:, :, 0:D],
                            rsum[:, lo:hi].unsqueeze(2).to_broadcast([P, hi - lo, D]), ALU.mult)
                        ins.then_inc(scaled, 1)
                    dve.wait_ge(scaled, (ib + 1) * OBANKS)
                    dve.sem_inc(acc_free, 1)
                    dve.wait_ge(resid_here, (ib + 1) * 16)
                    v.tensor_tensor(result[:, :, :], result[:, :, :], resid[:, :, :], ALU.add)\
                     .then_inc(result_ready, 1)
                    v.tensor_scalar(inlo[:, :], rsum[:, :], HI, None, ALU.is_le).then_inc(range_step, 1)
                    dve.wait_ge(range_step, ib * 3 + 4)
                    v.scalar_tensor_tensor(inrange[:, :], rsum[:, :], LO, inlo[:, :], ALU.is_ge, ALU.mult)\
                     .then_inc(range_step, 1)
                    dve.wait_ge(range_step, ib * 3 + 5)
                    v.tensor_tensor(fine[:, :], fine[:, :], inrange[:, :], ALU.mult).then_inc(range_step, 1)

        @block.tensor
        def _(pe):
            mm = nc.tensor.matmul
            pe.sem_inc(xn_free, 2)
            pe.sem_inc(step_free, SLOTS)
            pe.sem_inc(tb_filled, RAW * 2 * JT)
            pe.sem_inc(p_free, RING)
            pe.wait_ge(consts_ready, 2)
            pe.wait_ge(w_here, 32)
            for m in range(2):
                for k in range(CK):
                    for o in range(CK):
                        nc.tensor.transpose(flip[m][:, k * C + o * P:k * C + (o + 1) * P],
                                            wsb[:, m, o, k * P:(k + 1) * P], eye[:, :])
            pe.wait_ge(amat_ready, 1)
            for k in range(CK):
                for o in range(CK):
                    ins = mm(projA[0][:, k * 2 * H:(k + 1) * 2 * H], wsb[:, 0, o, k * P:(k + 1) * P],
                             amat[:, o, :], start=(o == 0), stop=(o == CK - 1))
            ins.then_inc(wT_done, 1)
            pe.wait_ge(wT_kept, CK)
            with pe.Fori(0, T // 2) as it:
                for k in range(2):
                    t = it * 2 + k
                    pe.wait_ge(xn_ready, t + 1)
                    for c in range(CK):
                        ins = nc.tensor.transpose(flip[k][:, c * P:(c + 1) * P], xn[:, k, c * P:(c + 1) * P],
                                                  eye[:, :])
                    ins.then_inc(flip_done, 1)
                    pe.wait_ge(flip_done, t + 1)
                    pe.sem_inc(xn_free, 1)
                    pe.wait_ge(hnT_ready, t + 1)
                    pe.wait_ge(proj_read, t + 1)
                    for c in range(CK):
                        mm(projA[k][:, 0:C + 2 * H], hnT[:, k, c, :], wall[:, c, 0:C + 2 * H],
                           start=(c == 0), stop=(c == CK - 1))
                    for c in range(CK):
                        mm(projB[k][:, 0:C], hnT[:, k, c, :], wall[:, c, C + 2 * H:],
                           start=(c == 0), stop=(c == CK - 1))
                    for c in range(CK):
                        ins = mm(projB[k][0:H, C:C + P], wall[:, c, C + H:C + 2 * H], hnT[:, k, c, :],
                                 start=(c == 0), stop=(c == CK - 1))
                    ins.then_inc(proj_done, 1)

            def flip_half(q, s, n):
                j, half = n // 2, n % 2
                pe.wait_ge(tb_free, q * (2 * JT) + n + 1)
                for c in range(4):
                    ins = nc.tensor.transpose(TB[n % 2][:, c * P:(c + 1) * P],
                                              raw[:, s % RAW, half * 4 + c, j * P:(j + 1) * P], eye[:, :])
                ins.then_inc(tb_filled, 1)

            pe.wait_ge(tab_ready, T)
            pe.wait_ge(masked, 1)
            for n in range(2 * JT):
                flip_half(0, 0, n)
            with pe.Fori(0, NIB) as ib:
                pe.wait_ge(acc_free, ib + 1)
                for k in range(OBANKS):
                    mm(OB[k][:, :], zeros[:, 0:P], zeros[:, :], start=True, stop=False, skip_group_check=True)
                with pe.Fori(0, NQ // SLOTS) as it:
                    g = ib * (NQ // SLOTS) + it
                    for s in range(SLOTS):
                        q = g * SLOTS + s
                        pe.wait_ge(masked, q + 2)
                        for h in range(H):
                            w = s * U + h
                            if h < 2 * JT:
                                flip_half(q + 1, (s + 1) % SLOTS, h)
                            pe.wait_ge(p_ready, g * (SLOTS * U) + w + 1)
                            for j in range(JT):
                                for n in range(NI):
                                    ins = mm(block_ap(n * H + h), ps[:, w % RING, j, n * P:(n + 1) * P],
                                             table[:, s, j, h * HW:(h + 1) * HW], start=False, stop=False,
                                             skip_group_check=True)
                            ins.then_inc(p_free, 1)
                        pe.wait_ge(p_free, q * U + U + RING)
                        pe.sem_inc(step_free, 1)


_INS = ['x', 'adj', 'L0_gnn_W', 'L0_gnn_We', 'L0_gnn_be', 'L0_gnn_a_src', 'L0_gnn_a_dst', 'L0_gnn_Wr', 'L0_gnn_br']
_OUTS = [((N, C), 'float32')]


def kernel(**inputs):
    import numpy as _np
    import concourse.bacc as _bacc
    from concourse import mybir as _mybir
    from concourse.bass_utils import run_bass_kernel_spmd as _run

    nc = _bacc.Bacc("TRN2", target_bir_lowering=False, num_devices=1)
    arrays, args = {}, []
    for name in _INS:
        a = _np.ascontiguousarray(inputs[name])
        arrays[f"in_{name}_dram"] = a
        args.append(nc.dram_tensor(f"in_{name}_dram", a.shape, _mybir.dt.from_np(a.dtype), kind="ExternalInput").ap())
    for i, (shape, dtype) in enumerate(_OUTS):
        dt = _mybir.dt.from_np(_np.dtype(dtype))
        args.append(nc.dram_tensor(f"out_{i}_dram", shape, dt, kind="ExternalOutput").ap())
    gat_layer(nc, *args)
    r = _run(nc, [arrays], core_ids=[0])
    return r.results[0]["out_0_dram"]
```

```python
import concourse.bass as bass
from concourse import mybir
from contextlib import ExitStack

F32 = mybir.dt.float32
BF16 = mybir.dt.bfloat16
I32 = mybir.dt.int32
ALU = mybir.AluOpType
ACT = mybir.ActivationFunctionType
AX = mybir.AxisListType
RMAX = bass.bass_isa.ReduceOp.max

P = 128
N, C = 8192, 256
H, D = 8, 32
CK = C // P
SLOPE = 0.2
RATIO = SLOPE / (1.0 - SLOPE)
EPS = 1e-5
T = N // P
XL = 8

IB = 1024
NIB = N // IB
NI = IB // P
JT = 2
JC = JT * P
NQ = N // JC
SLOTS = 4
RAW = 2
HALVES = 4 * JT
PR = 8
U = H

HW = D + 3
HX = H * HW + H
BIG = 2.0 ** 100
TINY = 2.0 ** -70
LO, HI = 1e-30, 1e25
HB = IB // 512
G = P // D


def gat_layer(nc, x, adj, W, We, be, a_src, a_dst, Wr, br, out):
    ctx = ExitStack()
    with ctx:
        def sb(name, shape, dt=F32):
            return ctx.enter_context(nc.sbuf_tensor(name, shape, dt))

        def sem(name):
            return ctx.enter_context(nc.semaphore(name))

        table_dram = nc.dram_tensor("table_dram", [N, HX], F32).ap()
        resid_dram = nc.dram_tensor("resid_dram", [N, C], F32).ap()
        ssrc_dram = nc.dram_tensor("ssrc_dram", [H, N], F32).ap()

        raw = sb("raw", [P, RAW, NI, JC])
        pen = sb("pen", [P, NI, JC], BF16)
        adjT = sb("adjT", [P, 2, 2, JT, IB])
        ps = sb("ps", [P, PR, JT, IB])
        srow = sb("srow", [P, H, IB])
        table = sb("table", [P, SLOTS, JT, HX])
        resid = sb("resid", [P, NI, C])
        result = sb("result", [P, NI, C])
        sums = sb("sums", [P, H // G + 1, IB])
        rsum = sb("rsum", [P, NI * H])
        inlo = sb("inlo", [P, NI * H])
        inrange = sb("inrange", [P, NI * H])
        fine = sb("fine", [P, NI * H])
        eye = sb("eye", [P, P])
        zeros = sb("zeros", [P, 512], BF16)
        minus_eye = sb("minus_eye", [P, P])
        eye_bf = sb("eye_bf", [P, P], BF16)
        w_mag = sb("w_mag", [P, H])
        w_scale = sb("w_scale", [P, H])
        w_over = sb("w_over", [P, H])
        w_neg = sb("w_neg", [P, H], I32)
        be_all = sb("be_all", [P, H])
        tmax = sb("tmax", [P, H])
        smin = sb("smin", [P, H])
        ends = sb("ends", [P, 2 * H])
        ends_all = sb("ends_all", [P, 2 * H])
        slope_t = sb("slope_t", [P, H])
        low = sb("low", [P, H])
        high = sb("high", [P, H])
        shift = sb("shift", [P, H])

        xs = ps[:, :, :, :].rearrange("p s j i -> p (s j i)").rearrange("p (t c) -> p t c", c=C)
        pool = srow[:, :, :].rearrange("p h i -> p (h i)")
        used = [0]

        def part(n):
            used[0] += n
            assert used[0] <= H * IB
            return pool[:, used[0] - n:used[0]]

        wsb = part(2 * CK * C).rearrange("p (m o k) -> p m o k", m=2, o=CK)
        amat = part(CK * 2 * H).rearrange("p (o m) -> p o m", o=CK)
        acol = part(CK * 2).rearrange("p (o m) -> p o m", o=CK)
        wall = part(CK * (2 * C + 2 * H)).rearrange("p (k n) -> p k n", k=CK)
        br_all = part(C)
        w_all = part(H)
        w_abs = part(H)
        w_col = part(1)
        w_col_abs = part(1)
        w_col_mag = part(1)
        w_col_inv = part(1)
        w_col_over = part(1)
        stats = part(T * 6).rearrange("p (t s) -> p t s", s=6)
        mv = part(T * 2).rearrange("p (t s) -> p t s", s=2)
        rstd = part(T)
        nmr = part(T)
        xn = part(2 * C).rearrange("p (s c) -> p s c", s=2)
        xb = part(2 * C).rearrange("p (s c) -> p s c", s=2)
        hnT = part(2 * CK * P).rearrange("p (s k i) -> p s k i", s=2, k=CK)
        tt = part(2 * H).rearrange("p (s h) -> p s h", s=2)
        et = part(2 * H).rearrange("p (s h) -> p s h", s=2)
        tab = part(2 * HX).rearrange("p (s n) -> p s n", s=2)
        rs = part(2 * C).rearrange("p (s c) -> p s c", s=2)
        ssT = part(2 * P).rearrange("p (s c) -> p s c", s=2)

        banks = [ctx.enter_context(nc.psum_tensor(f"bank{i}", [P, 512], F32)) for i in range(8)]
        NUM = [banks[0:HB], banks[HB:2 * HB]]
        DEN = banks[2 * HB:3 * HB]
        TB = banks[6:8]
        flip, projA, projB = banks[0:2], banks[2:4], banks[4:6]

        consts_ready = sem("consts_ready")
        eye_zero = sem("eye_zero")
        amat_zero = sem("amat_zero")
        tab_zero = sem("tab_zero")
        w_here = sem("w_here")
        small_here = sem("small_here")
        x_here = [sem(f"x_here{g}") for g in range(XL)]
        amat_ready = sem("amat_ready")
        wsgn_step = sem("wsgn_step")
        wT_done = sem("wT_done")
        wT_kept = sem("wT_kept")
        stat_done = sem("stat_done")
        aggr_done = sem("aggr_done")
        rstd_done = sem("rstd_done")
        norm_ready = sem("norm_ready")
        xn_ready = sem("xn_ready")
        xb_ready = sem("xb_ready")
        xn_free = sem("xn_free")
        flip_done = sem("flip_done")
        hnT_ready = sem("hnT_ready")
        proj_done = sem("proj_done")
        proj_read = sem("proj_read")
        t_ready = sem("t_ready")
        et_ready = sem("et_ready")
        tab_ready = sem("tab_ready")
        stored = sem("stored")
        smax_step = sem("smax_step")
        smax_ready = sem("smax_ready")
        smax_spread = sem("smax_spread")
        shift_step = sem("shift_step")
        shift_ready = sem("shift_ready")
        adj_here = [sem(f"adj_here{s}") for s in range(RAW)]
        table_here = [sem(f"table_here{s}") for s in range(SLOTS)]
        step_free = sem("step_free")
        pen_ready = sem("pen_ready")
        tb_filled = sem("tb_filled")
        kept = sem("kept")
        srow_here = [sem(f"srow_here{h}") for h in range(H)]
        resid_here = sem("resid_here")
        max_ready = sem("max_ready")
        sum_ready = sem("sum_ready")
        p_ready = sem("p_ready")
        p_free = sem("p_free")
        sums_kept = sem("sums_kept")
        sums_turned = sem("sums_turned")
        rsum_ready = sem("rsum_ready")
        scaled = sem("scaled")
        result_ready = sem("result_ready")
        range_step = sem("range_step")
        out_done = sem("out_done")

        block = ctx.enter_context(nc.Block())

        @block.sync
        def _(sp):
            sp.dma_start(wsb[:, 0], W.rearrange("(o p) k -> p o k", p=P)).then_inc(w_here, 16)
            sp.dma_start(wsb[:, 1], Wr.rearrange("(o p) k -> p o k", p=P)).then_inc(w_here, 16)
            sp.dma_start(acol[:, :, 0], a_dst.rearrange("(o g) d -> (g d) o", o=CK),
                         allow_slow_non_contiguous=True).then_inc(small_here, 16)
            sp.dma_start(acol[:, :, 1], a_src.rearrange("(o g) d -> (g d) o", o=CK),
                         allow_slow_non_contiguous=True).then_inc(small_here, 16)
            sp.dma_start(w_all[:, :], We.rearrange("h a -> a h").partition_broadcast(P)).then_inc(small_here, 16)
            sp.dma_start(w_col[0:H, :], We).then_inc(small_here, 16)
            sp.dma_start(be_all[:, :], be.partition_broadcast(P)).then_inc(small_here, 16)
            sp.dma_start(br_all[:, :], br.partition_broadcast(P)).then_inc(small_here, 16)
            for g in range(XL):
                n = T // XL
                sp.dma_start(xs[:, g * n:(g + 1) * n, :],
                             x[g * n * P:(g + 1) * n * P, :].rearrange("(t p) c -> p t c", p=P)).then_inc(x_here[g], 16)
            with sp.Fori(0, T // 2) as it:
                for k in range(2):
                    t = it * 2 + k
                    sp.wait_ge(tab_ready, t + 1)
                    sp.dma_start(table_dram[bass.ds(t * P, P), :], tab[:, k, :]).then_inc(stored, 16)
                    sp.dma_start(resid_dram[bass.ds(t * P, P), :], rs[:, k, :]).then_inc(stored, 16)
                    sp.dma_start(ssrc_dram[:, bass.ds(t * P, P)], ssT[0:H, k, :]).then_inc(stored, 16)
            sp.wait_ge(stored, 16 * 3 * T + 16)

            def load_adj(ib, jq, q, s):
                sp.wait_ge(tb_filled, (q + 1) * HALVES)
                sp.dma_start(raw[:, s % RAW], adj[bass.ds(ib * IB, IB), bass.ds(jq * JC, JC)]
                             .rearrange("(n p) j -> p n j", p=P)).then_inc(adj_here[s % RAW], 16)

            def load_table(jq, q, s):
                sp.wait_ge(step_free, q + 1)
                sp.dma_start(table[:, s], table_dram[bass.ds(jq * JC, JC), :]
                             .rearrange("(n p) c -> p n c", p=P)).then_inc(table_here[s], 16)

            with sp.Fori(0, NIB) as ib:
                with sp.Fori(0, NQ // SLOTS) as it:
                    for s in range(SLOTS):
                        load_adj(ib, it * SLOTS + s, ib * NQ + it * SLOTS + s, s)
                        load_table(it * SLOTS + s, ib * NQ + it * SLOTS + s, s)
            load_adj(0, 0, NIB * NQ, 0)
            sp.wait_ge(adj_here[0], (NIB * NQ // RAW + 1) * 16)
            for h in range(H):
                sp.wait_ge(srow_here[h], (NIB + 1) * 16)
            sp.wait_ge(out_done, 16 * NIB + 16)

        @block.gpsimd
        def _(gp):
            gp.memset(eye[:, :], 0.0).then_inc(eye_zero, 1)
            gp.memset(zeros[:, :], 0.0).then_inc(consts_ready, 1)
            gp.memset(minus_eye[:, :], 0.0).then_inc(eye_zero, 1)
            gp.memset(eye_bf[:, :], 0.0).then_inc(eye_zero, 1)
            gp.memset(amat[:, :, :], 0.0).then_inc(amat_zero, 1)
            gp.memset(tab[:, :, :], 0.0).then_inc(tab_zero, 1)
            gp.wait_ge(eye_zero, 3)
            for m, one in ((eye, 1.0), (minus_eye, -1.0), (eye_bf, 1.0)):
                gp.affine_select(out=m[:, :], in_=m[:, :], compare_op=ALU.not_equal, fill=one, base=0,
                                 pattern=[[-1, P]], channel_multiplier=1).then_inc(consts_ready, 1)
            for g in range(XL):
                gp.wait_ge(x_here[g], 16)
            gp.wait_ge(small_here, 16 * 6)
            with gp.Fori(0, T // 2) as it:
                for k in range(2):
                    t = it * 2 + k
                    gp.wait_ge(proj_read, t + 1)
                    gp.tensor_tensor(xb[:, k, :], xs[:, bass.ds(t, 1), :].rearrange("p a c -> p (a c)"),
                                     br_all[:, :], ALU.add).then_inc(xb_ready, 1)
            gp.wait_ge(smax_ready, 1)
            gp.partition_all_reduce(ends_all[:, :], ends[:, :], P, RMAX).then_inc(smax_spread, 1)

        @block.scalar
        def _(act):
            act.wait_ge(wT_done, 1)
            for k in range(CK):
                nc.scalar.activation(wall[:, k, 0:C], flip[0][:, k * C:(k + 1) * C], ACT.Copy)
                nc.scalar.activation(wall[:, k, C + 2 * H:], flip[1][:, k * C:(k + 1) * C], ACT.Copy)
                nc.scalar.activation(wall[:, k, C:C + 2 * H], projA[0][:, k * 2 * H:(k + 1) * 2 * H],
                                     ACT.Copy).then_inc(wT_kept, 1)
            act.wait_ge(rstd_done, 1)
            nc.scalar.activation(rstd[:, :], nmr[:, :], ACT.Sqrt).then_inc(rstd_done, 1)
            act.wait_ge(norm_ready, 1)

            def normal(t, k):
                act.wait_ge(xn_free, t + 1)
                act.wait_ge(norm_ready, 1)
                if isinstance(t, int):
                    row, r, m = xs[:, t, :], rstd[:, t:t + 1], nmr[:, t:t + 1]
                else:
                    row = xs[:, bass.ds(t, 1), :].rearrange("p a c -> p (a c)")
                    r, m = rstd[:, bass.ds(t, 1)], nmr[:, bass.ds(t, 1)]
                nc.scalar.activation(xn[:, k, :], row, ACT.Relu, bias=m, scale=r).then_inc(xn_ready, 1)

            def flipped(t, k):
                act.wait_ge(proj_read, t + 1)
                act.wait_ge(flip_done, t + 1)
                nc.scalar.activation(hnT[:, k], flip[k][:, 0:C].rearrange("p (k i) -> p k i", k=CK),
                                     ACT.Copy).then_inc(hnT_ready, 1)

            def factor(t, k):
                act.wait_ge(t_ready, t + 1)
                nc.scalar.activation(et[:, k, :], tt[:, k, :], ACT.Exp).then_inc(et_ready, 1)

            normal(0, 0)
            normal(1, 1)
            flipped(0, 0)
            with act.Fori(0, T // 2 - 1) as it:
                for k in range(2):
                    normal(it * 2 + k + 2, k)
                    flipped(it * 2 + k + 1, 1 - k)
                    factor(it * 2 + k, k)
            flipped(T - 1, 1)
            factor(T - 2, 0)
            factor(T - 1, 1)
            act.wait_ge(stored, 16 * 3 * T + 16)
            act.wait_ge(xn_ready, T)
            act.wait_ge(xb_ready, T)

            def load_srow(ib, h):
                act.dma_start(srow[:, h:h + 1, :], ssrc_dram[h:h + 1, bass.ds(ib * IB, IB)].partition_broadcast(P))\
                   .then_inc(srow_here[h], 16)

            def load_resid(ib):
                act.dma_start(resid[:, :, :], resid_dram[bass.ds(ib * IB, IB), :]
                              .rearrange("(n p) c -> p n c", p=P)).then_inc(resid_here, 16)

            def store_result(ib):
                act.wait_ge(result_ready, ib + 1)
                act.dma_start(out[bass.ds(ib * IB, IB), :].rearrange("(n p) c -> p n c", p=P),
                              result[:, :, :]).then_inc(out_done, 16)

            for h in range(H):
                load_srow(0, h)
            load_resid(0)
            act.wait_ge(shift_ready, 1)

            def keep(q, a, n):
                sign, j, half = n // (2 * JT), n // 2 % JT, n % 2
                act.wait_ge(tb_filled, q * HALVES + n + 1 + RAW * HALVES)
                nc.scalar.activation(adjT[:, a, sign, j, half * 512:half * 512 + 512], TB[n % 2][:, :],
                                     ACT.Copy).then_inc(kept, 1)

            def exp(q, h):
                act.wait_ge(sum_ready, q * U + h + 1)
                nc.scalar.activation(ps[:, h], ps[:, h], ACT.Exp, bias=shift[:, h:h + 1],
                                     scale=w_scale[:, h:h + 1]).then_inc(p_ready, 1)

            def keep_sums(ib):
                act.wait_ge(p_free, (ib + 1) * (NQ * U) + PR)
                for n, bank in enumerate(NUM[0] + NUM[1] + DEN):
                    ins = nc.scalar.activation(sums[:, n // HB, n % HB * 512:(n % HB + 1) * 512], bank[:, :],
                                               ACT.Copy)
                ins.then_inc(sums_kept, 1)

            def group(ib, it, end=False, before=None):
                for s in range(SLOTS):
                    q = ib * NQ + it * SLOTS + s
                    for h in range(H):
                        exp(q, h)
                        if before is not None and s == 0 and h == 0:
                            keep_sums(before)
                        if end and s == SLOTS - 1:
                            load_srow((ib + 1) % NIB, h)
                        for n in range(2 * h, min(2 * h + 2, HALVES)):
                            keep(q + 1, (s + 1) % 2, n)

            last = NQ // SLOTS - 1
            for n in range(HALVES):
                keep(0, 0, n)
            group(0, 0)
            with act.Fori(0, NIB - 1) as ib:
                with act.Fori(1, last) as it:
                    group(ib, it)
                group(ib, last, end=True)
                group(ib + 1, 0, before=ib)
                store_result(ib)
                load_resid(ib + 1)
            with act.Fori(1, last) as it:
                group(NIB - 1, it)
            group(NIB - 1, last, end=True)
            keep_sums(NIB - 1)
            store_result(NIB - 1)

        @block.vector
        def _(dve):
            v = nc.vector
            dve.sem_inc(proj_read, 2)
            dve.sem_inc(scaled, 4 * HB)
            dve.sem_inc(stored, 16)
            dve.sem_inc(out_done, 16)
            dve.sem_inc(range_step, 3)
            v.memset(fine[:, :], 1.0)
            v.memset(tmax[:, :], -3.0e38)
            v.memset(smin[:, :], 3.0e38).then_inc(smax_step, 1)
            dve.wait_ge(small_here, 16 * 6)
            dve.wait_ge(amat_zero, 1)
            for o in range(CK):
                for g in range(P // D):
                    for m in range(2):
                        h = o * (P // D) + g
                        ins = v.tensor_copy(amat[g * D:(g + 1) * D, o, m * H + h:m * H + h + 1],
                                            acol[g * D:(g + 1) * D, o, m:m + 1])
            ins.then_inc(amat_ready, 1)
            v.tensor_scalar(w_neg[:, :], w_all[:, :], 0.0, None, ALU.is_lt)
            v.scalar_tensor_tensor(w_col_abs[0:H, :], w_col[0:H, :], -1.0, w_col[0:H, :], ALU.mult, ALU.max)
            v.scalar_tensor_tensor(w_abs[:, :], w_all[:, :], -1.0, w_all[:, :], ALU.mult, ALU.max)\
             .then_inc(wsgn_step, 1)
            dve.wait_ge(wsgn_step, 1)
            v.tensor_scalar(w_col_mag[0:H, :], w_col_abs[0:H, :], TINY, None, ALU.max)
            v.tensor_scalar(w_mag[:, :], w_abs[:, :], TINY, None, ALU.max).then_inc(wsgn_step, 1)
            dve.wait_ge(wsgn_step, 2)
            v.tensor_scalar(w_scale[:, :], w_mag[:, :], 1.0 - SLOPE, None, ALU.mult)
            v.reciprocal(w_col_inv[0:H, :], w_col_mag[0:H, :])
            v.reciprocal(w_abs[:, :], w_mag[:, :]).then_inc(wsgn_step, 1)
            dve.wait_ge(wsgn_step, 3)
            v.tensor_scalar(w_col_over[0:H, :], w_col_inv[0:H, :], -1.0, None, ALU.mult)
            v.tensor_scalar(w_over[:, :], w_abs[:, :], -1.0, None, ALU.mult).then_inc(wsgn_step, 1)
            dve.wait_ge(wsgn_step, 4)
            for t in range(T):
                if t % (T // XL) == 0:
                    dve.wait_ge(x_here[t // (T // XL)], 16)
                v.bn_stats(stats[:, t, :], xs[:, t, :]).then_inc(stat_done, 1)
            for t in range(T):
                dve.wait_ge(stat_done, t + 1)
                v.bn_aggr(mv[:, t, :], stats[:, t, :]).then_inc(aggr_done, 1)
            dve.wait_ge(aggr_done, T)
            v.tensor_scalar(nmr[:, :], mv[:, :, 1], EPS, None, ALU.add).then_inc(rstd_done, 1)
            dve.wait_ge(rstd_done, 2)
            v.reciprocal(rstd[:, :], rstd[:, :]).then_inc(rstd_done, 1)
            dve.wait_ge(rstd_done, 3)
            v.scalar_tensor_tensor(nmr[:, :], mv[:, :, 0], -1.0, rstd[:, :], ALU.mult, ALU.mult)\
             .then_inc(norm_ready, 1)

            def rest(t, k):
                dve.wait_ge(proj_done, t + 1)
                v.tensor_tensor(tt[:, k, :], projA[k][:, C:C + H], be_all[:, :], ALU.add).then_inc(t_ready, 1)
                dve.wait_ge(smax_step, t + 1)
                v.tensor_tensor(smin[:, :], projA[k][:, C + H:C + 2 * H], smin[:, :], ALU.min)
                v.tensor_tensor(tmax[:, :], projA[k][:, C:C + H], tmax[:, :], ALU.max).then_inc(smax_step, 1)
                dve.wait_ge(stored, 48 * t + 16)
                v.tensor_scalar(ssT[0:H, k, :], projB[k][0:H, C:C + P], w_col_over[0:H, :], None, ALU.mult)
                dve.wait_ge(xb_ready, t + 1)
                v.tensor_tensor(rs[:, k, :], projB[k][:, 0:C], xb[:, k, :], ALU.add)
                dve.wait_ge(t_ready, t + 1)
                v.tensor_tensor(tab[:, k, H * HW:], tt[:, k, :], w_over[:, :], ALU.mult)

            def heads(t, k):
                dve.wait_ge(et_ready, t + 1)
                rows = tab[:, k, 0:H * HW].rearrange("p (h d) -> p h d", h=H)
                v.tensor_copy(rows[:, :, D + 1], et[:, k, :])
                v.tensor_tensor(rows[:, :, 0:D], projA[k][:, 0:C].rearrange("p (h d) -> p h d", h=H),
                                et[:, k, :].unsqueeze(2).to_broadcast([P, H, D]), ALU.mult).then_inc(tab_ready, 1)
                dve.wait_ge(tab_ready, t + 1)
                dve.sem_inc(proj_read, 1)

            dve.wait_ge(tab_zero, 1)
            rest(0, 0)
            with dve.Fori(0, T // 2 - 1) as it:
                heads(it * 2, 0)
                rest(it * 2 + 1, 1)
                heads(it * 2 + 1, 1)
                rest(it * 2 + 2, 0)
            heads(T - 2, 0)
            rest(T - 1, 1)
            heads(T - 1, 1)
            dve.wait_ge(smax_step, T + 1)
            v.tensor_scalar(ends[:, H:], smin[:, :], -1.0, None, ALU.mult)
            v.tensor_tensor(ends[:, 0:H], tmax[:, :], be_all[:, :], ALU.add).then_inc(smax_ready, 1)
            dve.wait_ge(smax_spread, 1)
            v.tensor_scalar(slope_t[:, :], ends_all[:, 0:H], SLOPE, None, ALU.mult).then_inc(shift_step, 1)
            dve.wait_ge(shift_step, 1)
            v.scalar_tensor_tensor(low[:, :], ends_all[:, H:], 1.0 - SLOPE, slope_t[:, :], ALU.mult, ALU.add)\
             .then_inc(shift_step, 1)
            dve.wait_ge(shift_step, 2)
            v.tensor_tensor(high[:, :], low[:, :], ends_all[:, 0:H], ALU.max).then_inc(shift_step, 1)
            dve.wait_ge(shift_step, 3)
            v.tensor_scalar(shift[:, :], high[:, :], -1.0, None, ALU.mult).then_inc(shift_ready, 1)

            which = [v.value_load(w_neg[0:1, h:h + 1], min_val=0, max_val=1) for h in range(H)]

            def penalise(q, s):
                dve.wait_ge(adj_here[s % RAW], q * (16 // RAW) + 16 - (s % RAW) * (16 // RAW))
                if not (isinstance(q, int) and q == 0):
                    dve.wait_ge(tb_filled, q * HALVES + RAW * HALVES)
                v.tensor_scalar(pen[:, :, :], raw[:, s % RAW], 0.0, -BIG, ALU.is_le, ALU.mult).then_inc(pen_ready, 1)

            def signed(s, h):
                return adjT[:, s % 2, bass.ds(which[h], 1)].rearrange("p a j i -> p (a j) i")

            def maximum(q, s, h):
                dve.wait_ge(p_free, q * U + h + 1)
                for j in range(JT):
                    ins = v.scalar_tensor_tensor(
                        ps[:, h, j], srow[:, h, :], table[:, s, j, H * HW + h:H * HW + h + 1],
                        adjT[:, s % 2, bass.ds(which[h], 1), j, :].rearrange("p a i -> p (a i)"), ALU.add, ALU.max)
                ins.then_inc(max_ready, 1)

            def exponent(q, s, h):
                dve.wait_ge(max_ready, q * U + h + 1)
                v.scalar_tensor_tensor(ps[:, h], signed(s, h), RATIO, ps[:, h], ALU.mult, ALU.add)\
                 .then_inc(sum_ready, 1)

            def finish(ib):
                dve.wait_ge(sums_turned, ib + 1)
                dve.wait_ge(range_step, ib * 3 + 3)
                for b in range(HB):
                    n = NI // HB * H
                    den = DEN[b][:, :].rearrange("p (n g x) -> p n x g", n=NI // HB, g=G)[:, :, 0:H // G, :]
                    v.reciprocal(rsum[:, b * n:(b + 1) * n].rearrange("p (n r g) -> p n r g", r=H // G, g=G), den)\
                     .then_inc(rsum_ready, 1)
                dve.wait_ge(out_done, ib * 16 + 16)
                dve.wait_ge(rsum_ready, (ib + 1) * HB)
                for k, bank in enumerate(NUM[0] + NUM[1]):
                    rows = result[:, 2 * k:2 * k + 2, :].rearrange("p n (r g d) -> p (n r) g d", g=G, d=D)
                    acc = bank[:, :].rearrange("p (m g d) -> p m g d", g=G, d=D)
                    over = rsum[:, k * 2 * H:(k + 1) * 2 * H].rearrange("p (m g) -> p m g", g=G)
                    for g in (0, 2):
                        v.tensor_tensor(rows[:, :, g:g + 2, :], acc[:, :, g:g + 2, :],
                                        over[:, :, (g + 2) % G:(g + 2) % G + 2].unsqueeze(3)
                                        .to_broadcast([P, 4, 2, D]), ALU.mult).then_inc(scaled, 1)
                v.tensor_scalar(inlo[:, :], rsum[:, :], HI, None, ALU.is_le).then_inc(range_step, 1)
                dve.wait_ge(range_step, ib * 3 + 4)
                v.scalar_tensor_tensor(inrange[:, :], rsum[:, :], LO, inlo[:, :], ALU.is_ge, ALU.mult)\
                 .then_inc(range_step, 1)
                dve.wait_ge(range_step, ib * 3 + 5)
                v.tensor_tensor(fine[:, :], fine[:, :], inrange[:, :], ALU.mult).then_inc(range_step, 1)
                dve.wait_ge(scaled, (ib + 2) * 4 * HB)
                dve.wait_ge(resid_here, (ib + 1) * 16)
                v.tensor_tensor(result[:, :, :], result[:, :, :], resid[:, :, :], ALU.add).then_inc(result_ready, 1)

            def group(ib, it, start=False, first=False, finishing=None):
                for s in range(SLOTS):
                    q = ib * NQ + it * SLOTS + s
                    dve.wait_ge(table_here[s], q * (16 // SLOTS) + (16 - s * (16 // SLOTS)))
                    for h in range(H):
                        if h == 0:
                            dve.wait_ge(kept, (q + 2) * HALVES)
                        if first and s == 0:
                            dve.wait_ge(srow_here[h], ib * 16 + 16)
                        maximum(q, s, h)
                        if h:
                            exponent(q, s, h - 1)
                        elif not (start and s == 0):
                            exponent(q - 1, s - 1, U - 1)
                        if h == 0:
                            penalise(q + 1, s + 1)
                    if finishing is not None and s == 0:
                        finish(finishing)

            penalise(0, 0)
            group(0, 0, start=True, first=True)
            with dve.Fori(0, NIB - 1) as ib:
                with dve.Fori(1, NQ // SLOTS) as it:
                    group(ib, it)
                group(ib + 1, 0, first=True, finishing=ib)
            with dve.Fori(1, NQ // SLOTS) as it:
                group(NIB - 1, it)
            exponent(NIB * NQ - 1, SLOTS - 1, U - 1)
            finish(NIB - 1)

        @block.tensor
        def _(pe):
            mm = nc.tensor.matmul
            pe.sem_inc(xn_free, 2)
            pe.sem_inc(step_free, SLOTS - 1)
            pe.sem_inc(tb_filled, RAW * HALVES)
            pe.sem_inc(kept, HALVES)
            pe.sem_inc(p_free, PR)
            pe.wait_ge(consts_ready, 4)
            pe.wait_ge(w_here, 32)
            for m in range(2):
                for k in range(CK):
                    for o in range(CK):
                        nc.tensor.transpose(flip[m][:, k * C + o * P:k * C + (o + 1) * P],
                                            wsb[:, m, o, k * P:(k + 1) * P], eye[:, :])
            pe.wait_ge(amat_ready, 1)
            for k in range(CK):
                for o in range(CK):
                    ins = mm(projA[0][:, k * 2 * H:(k + 1) * 2 * H], wsb[:, 0, o, k * P:(k + 1) * P],
                             amat[:, o, :], start=(o == 0), stop=(o == CK - 1))
            ins.then_inc(wT_done, 1)
            pe.wait_ge(wT_kept, CK)

            def flip_x(t, k):
                pe.wait_ge(xn_ready, t + 1)
                for c in range(CK):
                    ins = nc.tensor.transpose(flip[k][:, c * P:(c + 1) * P], xn[:, k, c * P:(c + 1) * P], eye[:, :])
                ins.then_inc(flip_done, 1)

            def project(t, k):
                pe.wait_ge(hnT_ready, t + 1)
                pe.sem_inc(xn_free, 1)
                pe.wait_ge(proj_read, t + 1)
                for c in range(CK):
                    mm(projA[k][:, 0:C + 2 * H], hnT[:, k, c, :], wall[:, c, 0:C + 2 * H],
                       start=(c == 0), stop=(c == CK - 1))
                for c in range(CK):
                    mm(projB[k][:, 0:C], hnT[:, k, c, :], wall[:, c, C + 2 * H:],
                       start=(c == 0), stop=(c == CK - 1))
                for c in range(CK):
                    ins = mm(projB[k][0:H, C:C + P], wall[:, c, C + H:C + 2 * H], hnT[:, k, c, :],
                             start=(c == 0), stop=(c == CK - 1))
                ins.then_inc(proj_done, 1)

            flip_x(0, 0)
            with pe.Fori(0, T // 2 - 1) as it:
                for k in range(2):
                    flip_x(it * 2 + k + 1, 1 - k)
                    project(it * 2 + k, k)
            flip_x(T - 1, 1)
            project(T - 2, 0)
            project(T - 1, 1)

            def flip_half(q, s, n):
                sign, j, half = n // (2 * JT), n // 2 % JT, n % 2
                pe.wait_ge(kept, q * HALVES + n + 7)
                bank = TB[n % 2]
                for c in range(4):
                    at = slice(c * P, (c + 1) * P)
                    mm(bank[:, at], pen[:, half * 4 + c, j * P:(j + 1) * P], eye_bf[:, :],
                       start=True, stop=False, skip_group_check=True)
                    ins = mm(bank[:, at], raw[:, s % RAW, half * 4 + c, j * P:(j + 1) * P],
                             (minus_eye if sign else eye)[:, :], start=False, stop=True, skip_group_check=True)
                ins.then_inc(tb_filled, 1)

            pe.wait_ge(tab_ready, T)
            pe.wait_ge(pen_ready, 1)
            for n in range(HALVES):
                flip_half(0, 0, n)
            with pe.Fori(0, NIB) as ib:
                pe.wait_ge(scaled, (ib + 1) * 4 * HB)
                for bank in NUM[0] + NUM[1] + DEN:
                    mm(bank[:, :], zeros[:, 0:P], zeros[:, :], start=True, stop=False, skip_group_check=True)
                with pe.Fori(0, NQ // SLOTS) as it:
                    for s in range(SLOTS):
                        q = ib * NQ + it * SLOTS + s
                        for h in range(H):
                            if h == 0:
                                pe.wait_ge(pen_ready, q + 2)
                            for n in range(2 * h, min(2 * h + 2, HALVES)):
                                flip_half(q + 1, s + 1, n)
                            if h % 2:
                                pe.wait_ge(p_ready, q * U + h + 1)
                                for j in range(JT):
                                    for b in range(HB):
                                        at = slice(b * 512, (b + 1) * 512)
                                        for m in (h - 1, h):
                                            g = m % G * D
                                            mm(NUM[m // G][b][g:g + D, :], table[:, s, j, m * HW:m * HW + D],
                                               ps[:, m, j, at], start=False, stop=False, skip_group_check=True)
                                        for m in (h - 1, h):
                                            g = (m + 2) % G * D
                                            c = m * HW + D + (1 - m // G)
                                            ins = mm(DEN[b][g:g + 2, :], table[:, s, j, c:c + 2],
                                                     ps[:, m, j, at], start=False, stop=False, skip_group_check=True)
                                ins.then_inc(p_free, 2)
                            if h == 1:
                                pe.wait_ge(p_free, q * U + PR)
                                pe.sem_inc(step_free, 1)
                pe.wait_ge(sums_kept, ib + 1)
                for n in range(NI):
                    bank = (NUM[0] + NUM[1])[n // 2]
                    for r in range(H // G):
                        nc.tensor.transpose(bank[:, n % 2 * C + r * P:n % 2 * C + (r + 1) * P],
                                            sums[:, r, n * P:(n + 1) * P], eye[:, :])
                    b = n // (NI // HB)
                    ins = nc.tensor.transpose(DEN[b][:, n % (NI // HB) * P:(n % (NI // HB) + 1) * P],
                                              sums[:, H // G, n * P:(n + 1) * P], eye[:, :])
                ins.then_inc(sums_turned, 1)


_INS = ['x', 'adj', 'L0_gnn_W', 'L0_gnn_We', 'L0_gnn_be', 'L0_gnn_a_src', 'L0_gnn_a_dst', 'L0_gnn_Wr', 'L0_gnn_br']
_OUTS = [((N, C), 'float32')]


def kernel(**inputs):
    import numpy as _np
    import concourse.bacc as _bacc
    from concourse import mybir as _mybir
    from concourse.bass_utils import run_bass_kernel_spmd as _run

    nc = _bacc.Bacc("TRN2", target_bir_lowering=False, num_devices=1)
    arrays, args = {}, []
    for name in _INS:
        a = _np.ascontiguousarray(inputs[name])
        arrays[f"in_{name}_dram"] = a
        args.append(nc.dram_tensor(f"in_{name}_dram", a.shape, _mybir.dt.from_np(a.dtype), kind="ExternalInput").ap())
    for i, (shape, dtype) in enumerate(_OUTS):
        dt = _mybir.dt.from_np(_np.dtype(dtype))
        args.append(nc.dram_tensor(f"out_{i}_dram", shape, dt, kind="ExternalOutput").ap())
    gat_layer(nc, *args)
    r = _run(nc, [arrays], core_ids=[0])
    return r.results[0]["out_0_dram"]
```
